# Optimizing a Trainium2 kernel written in Bass

```python
import numpy as np
import jax
import jax.numpy as jnp

def _softmax(x, axis=-1):
    return jax.nn.softmax(x, axis=axis)

def _gelu(x):
    return jax.nn.gelu(x, approximate=True)

def _silu(x):
    return jax.nn.silu(x)

def _sigmoid(x):
    return jax.nn.sigmoid(x)

def _layernorm(x, axis=-1, eps=1e-05):
    m = jnp.mean(x, axis=axis, keepdims=True)
    v = jnp.var(x, axis=axis, keepdims=True)
    return (x - m) / jnp.sqrt(v + eps)

def _scatter_add(tgt, idx, src, axis=0):
    return tgt.at[idx].add(src)

def _segment_sum(src, seg, n):
    return jax.ops.segment_sum(src, seg, n)
kernel_name = 'mk_adaln_attn_ffn_d1_seqx_r8_4bf9a1'

def setup_inputs(seed: int=0):
    np.random.seed(seed)
    _w = jnp.asarray

    def _rec_inputs():
        import jax
        import jax.numpy as jnp
        _rk = jax.random.key(seed)
        x = -0.000125 + 0.9999 * jax.random.normal(jax.random.fold_in(_rk, 1), (4, 256, 256), jnp.float32)
        _lenS = 256 - jax.random.randint(jax.random.fold_in(_rk, 7), (4,), 0, max(1, 256 // 4) + 1, jnp.int32)
        _lenS2 = 256 - jax.random.randint(jax.random.fold_in(_rk, 8), (4,), 0, max(1, 256 // 4) + 1, jnp.int32)
        fside_BxSxS_0 = -1.52775e-05 + 0.999936 * jax.random.normal(jax.random.fold_in(_rk, 11), (4, 256, 256), jnp.float32)
        cond_512 = -5.03954e-05 + 1.00559 * jax.random.normal(jax.random.fold_in(_rk, 12), (4, 64), jnp.float32)
        return (x, fside_BxSxS_0, cond_512)
    x, fside_BxSxS_0, cond_512 = _rec_inputs()

    def _L0_cond_setup():
        import jax, jax.numpy as jnp
        from jax import lax
        import numpy as np
        B, T, C, TD = (8, 256, 256, 64)

        def _bi_wkv(r, k, v, w, u, time_emb):
            tf = jax.nn.sigmoid(jnp.sum(time_emb, axis=-1))[:, None, None]
            decay = jnp.exp(-jnp.exp(w.astype(jnp.float32)))[None, :] * (0.5 + 0.5 * tf[:, :, 0])
            kf = k.astype(jnp.float32)
            vf = v.astype(jnp.float32)
            ek = jnp.exp(jnp.minimum(kf, 30.0))
            ekv = ek * vf

            def step(carry, x):
                a, b = carry
                ekv_t, ek_t = x
                a = a * decay + ekv_t
                b = b * decay + ek_t
                return ((a, b), (a, b))
            ekv_t = jnp.swapaxes(ekv, 0, 1)
            ek_t = jnp.swapaxes(ek, 0, 1)
            init = (jnp.zeros_like(decay), jnp.zeros_like(decay))
            _, (nf, df) = lax.scan(step, init, (ekv_t, ek_t))
            _, (nb, db) = lax.scan(step, init, (ekv_t, ek_t), reverse=True)
            nf = jnp.swapaxes(nf, 0, 1)
            df = jnp.swapaxes(df, 0, 1)
            nb = jnp.swapaxes(nb, 0, 1)
            db = jnp.swapaxes(db, 0, 1)
            euk = jnp.exp(jnp.minimum(u.astype(jnp.float32)[None, None, :] + kf, 30.0))
            num = nf + nb - ekv + euk * vf
            den = df + db - ek + euk
            base = jax.nn.sigmoid(r.astype(jnp.float32)) * (num / jnp.maximum(den, 1e-08))
            out = base * (0.8 + 0.2 * tf)
            return out.astype(r.dtype)
        key = jax.random.key(seed)
        ks = jax.random.split(key, 6)
        return {'r': jax.random.normal(ks[0], (B, T, C), dtype=jnp.float32), 'k': jax.random.normal(ks[1], (B, T, C), dtype=jnp.float32), 'v': jax.random.normal(ks[2], (B, T, C), dtype=jnp.float32), 'w': jax.random.normal(ks[3], (C,), dtype=jnp.float32), 'u': jax.random.normal(ks[4], (C,), dtype=jnp.float32), 'time_emb': jax.random.normal(ks[5], (B, TD), dtype=jnp.float32)}
    _L0_cond_all = _L0_cond_setup()
    _L0_cond_in = {k: v for k, v in _L0_cond_all.items() if k in ('w', 'u')}
    del _L0_cond_all

    def _L0_attn_setup():
        import jax, jax.numpy as jnp
        import numpy as np
        B, T, D_MODEL = (2, 256, 256)
        N_HEADS, N_KV_HEADS, HEAD_DIM = (16, 4, 128)
        N_REP = N_HEADS // N_KV_HEADS
        EPS = 1e-06

        def _qknorm(t, scale):
            norm = jax.lax.rsqrt(jnp.mean(t * t, axis=-1, keepdims=True) + EPS)
            return t * norm * scale
        key = jax.random.key(seed)
        ks = jax.random.split(key, 5)
        return {'x': jax.random.normal(ks[0], (B, T, D_MODEL), dtype=jnp.float32), 'Wq': jax.random.normal(ks[1], (N_HEADS * HEAD_DIM, D_MODEL), dtype=jnp.float32) * 0.02, 'Wk': jax.random.normal(ks[2], (N_KV_HEADS * HEAD_DIM, D_MODEL), dtype=jnp.float32) * 0.02, 'Wv': jax.random.normal(ks[3], (N_KV_HEADS * HEAD_DIM, D_MODEL), dtype=jnp.float32) * 0.02, 'Wo': jax.random.normal(ks[4], (D_MODEL, N_HEADS * HEAD_DIM), dtype=jnp.float32) * 0.02, 'q_scale': jnp.ones((HEAD_DIM,), dtype=jnp.float32), 'k_scale': jnp.ones((HEAD_DIM,), dtype=jnp.float32)}
    _L0_attn_all = _L0_attn_setup()
    _L0_attn_in = {k: v for k, v in _L0_attn_all.items() if k in ('Wq', 'Wk', 'Wv', 'Wo', 'q_scale', 'k_scale')}
    del _L0_attn_all

    def _L0_cond2_setup():
        import jax, jax.numpy as jnp
        from jax import lax
        import numpy as np
        B, T, C, TD = (8, 256, 256, 64)

        def _bi_wkv(r, k, v, w, u, time_emb):
            tf = jax.nn.sigmoid(jnp.sum(time_emb, axis=-1))[:, None, None]
            decay = jnp.exp(-jnp.exp(w.astype(jnp.float32)))[None, :] * (0.5 + 0.5 * tf[:, :, 0])
            kf = k.astype(jnp.float32)
            vf = v.astype(jnp.float32)
            ek = jnp.exp(jnp.minimum(kf, 30.0))
            ekv = ek * vf

            def step(carry, x):
                a, b = carry
                ekv_t, ek_t = x
                a = a * decay + ekv_t
                b = b * decay + ek_t
                return ((a, b), (a, b))
            ekv_t = jnp.swapaxes(ekv, 0, 1)
            ek_t = jnp.swapaxes(ek, 0, 1)
            init = (jnp.zeros_like(decay), jnp.zeros_like(decay))
            _, (nf, df) = lax.scan(step, init, (ekv_t, ek_t))
            _, (nb, db) = lax.scan(step, init, (ekv_t, ek_t), reverse=True)
            nf = jnp.swapaxes(nf, 0, 1)
            df = jnp.swapaxes(df, 0, 1)
            nb = jnp.swapaxes(nb, 0, 1)
            db = jnp.swapaxes(db, 0, 1)
            euk = jnp.exp(jnp.minimum(u.astype(jnp.float32)[None, None, :] + kf, 30.0))
            num = nf + nb - ekv + euk * vf
            den = df + db - ek + euk
            base = jax.nn.sigmoid(r.astype(jnp.float32)) * (num / jnp.maximum(den, 1e-08))
            out = base * (0.8 + 0.2 * tf)
            return out.astype(r.dtype)
        key = jax.random.key(seed)
        ks = jax.random.split(key, 6)
        return {'r': jax.random.normal(ks[0], (B, T, C), dtype=jnp.float32), 'k': jax.random.normal(ks[1], (B, T, C), dtype=jnp.float32), 'v': jax.random.normal(ks[2], (B, T, C), dtype=jnp.float32), 'w': jax.random.normal(ks[3], (C,), dtype=jnp.float32), 'u': jax.random.normal(ks[4], (C,), dtype=jnp.float32), 'time_emb': jax.random.normal(ks[5], (B, TD), dtype=jnp.float32)}
    _L0_cond2_all = _L0_cond2_setup()
    _L0_cond2_in = {k: v for k, v in _L0_cond2_all.items() if k in ('w', 'u')}
    del _L0_cond2_all

    def _L0_ffn_setup():
        import jax, jax.numpy as jnp
        import numpy as np
        TOP_K = 8
        NEG_INF = -1000000000.0
        key = jax.random.key(seed)
        ks = jax.random.split(key, 6)
        B, S, H, I, E, G, GS = (1, 256, 256, 176, 64, 8, 8)
        sc = 0.02
        return {'hidden_states': jax.random.normal(ks[0], (B, S, H), jnp.float32), 'gate_w': jax.random.normal(ks[1], (E, H), jnp.float32) * sc, 'mask_up_w': jax.random.normal(ks[2], (G, H, GS), jnp.float32) * sc, 'gate_proj_w': jax.random.normal(ks[3], (G, I, H), jnp.float32) * sc, 'up_proj_w': jax.random.normal(ks[4], (G, I, H), jnp.float32) * sc, 'down_proj_w': jax.random.normal(ks[5], (G, H, I), jnp.float32) * sc, 'inv_map': jnp.arange(G * GS, dtype=jnp.int64).reshape(G, GS)}
    _L0_ffn_all = _L0_ffn_setup()
    _L0_ffn_in = {k: v for k, v in _L0_ffn_all.items() if k in ('gate_w', 'mask_up_w', 'gate_proj_w', 'up_proj_w', 'down_proj_w', 'inv_map')}
    del _L0_ffn_all
    return {'x': x, 'fside_BxSxS_0': fside_BxSxS_0, 'cond_512': cond_512, 'L0_cond_w': _L0_cond_in['w'], 'L0_cond_u': _L0_cond_in['u'], 'L0_attn_Wq': _L0_attn_in['Wq'], 'L0_attn_Wk': _L0_attn_in['Wk'], 'L0_attn_Wv': _L0_attn_in['Wv'], 'L0_attn_Wo': _L0_attn_in['Wo'], 'L0_attn_q_scale': _L0_attn_in['q_scale'], 'L0_attn_k_scale': _L0_attn_in['k_scale'], 'L0_cond2_w': _L0_cond2_in['w'], 'L0_cond2_u': _L0_cond2_in['u'], 'L0_ffn_gate_w': _L0_ffn_in['gate_w'], 'L0_ffn_mask_up_w': _L0_ffn_in['mask_up_w'], 'L0_ffn_gate_proj_w': _L0_ffn_in['gate_proj_w'], 'L0_ffn_up_proj_w': _L0_ffn_in['up_proj_w'], 'L0_ffn_down_proj_w': _L0_ffn_in['down_proj_w'], 'L0_ffn_inv_map': _L0_ffn_in['inv_map']}

def reference(x, fside_BxSxS_0, cond_512, L0_cond_w, L0_cond_u, L0_attn_Wq, L0_attn_Wk, L0_attn_Wv, L0_attn_Wo, L0_attn_q_scale, L0_attn_k_scale, L0_cond2_w, L0_cond2_u, L0_ffn_gate_w, L0_ffn_mask_up_w, L0_ffn_gate_proj_w, L0_ffn_up_proj_w, L0_ffn_down_proj_w, L0_ffn_inv_map):
    import jax
    import jax.numpy as jnp

    def _L0_cond_ref(r, k, v, w, u, time_emb):
        import jax, jax.numpy as jnp
        from jax import lax
        import numpy as np
        B, T, C, TD = (8, 256, 256, 64)

        def _bi_wkv(r, k, v, w, u, time_emb):
            tf = jax.nn.sigmoid(jnp.sum(time_emb, axis=-1))[:, None, None]
            decay = jnp.exp(-jnp.exp(w.astype(jnp.float32)))[None, :] * (0.5 + 0.5 * tf[:, :, 0])
            kf = k.astype(jnp.float32)
            vf = v.astype(jnp.float32)
            ek = jnp.exp(jnp.minimum(kf, 30.0))
            ekv = ek * vf

            def step(carry, x):
                a, b = carry
                ekv_t, ek_t = x
                a = a * decay + ekv_t
                b = b * decay + ek_t
                return ((a, b), (a, b))
            ekv_t = jnp.swapaxes(ekv, 0, 1)
            ek_t = jnp.swapaxes(ek, 0, 1)
            init = (jnp.zeros_like(decay), jnp.zeros_like(decay))
            _, (nf, df) = lax.scan(step, init, (ekv_t, ek_t))
            _, (nb, db) = lax.scan(step, init, (ekv_t, ek_t), reverse=True)
            nf = jnp.swapaxes(nf, 0, 1)
            df = jnp.swapaxes(df, 0, 1)
            nb = jnp.swapaxes(nb, 0, 1)
            db = jnp.swapaxes(db, 0, 1)
            euk = jnp.exp(jnp.minimum(u.astype(jnp.float32)[None, None, :] + kf, 30.0))
            num = nf + nb - ekv + euk * vf
            den = df + db - ek + euk
            base = jax.nn.sigmoid(r.astype(jnp.float32)) * (num / jnp.maximum(den, 1e-08))
            out = base * (0.8 + 0.2 * tf)
            return out.astype(r.dtype)
        return _bi_wkv(r, k, v, w, u, time_emb)

    def _L0_attn_ref(x, Wq, Wk, Wv, Wo, q_scale, k_scale):
        import jax, jax.numpy as jnp
        import numpy as np
        B, T, D_MODEL = (2, 256, 256)
        N_HEADS, N_KV_HEADS, HEAD_DIM = (16, 4, 128)
        N_REP = N_HEADS // N_KV_HEADS
        EPS = 1e-06

        def _qknorm(t, scale):
            norm = jax.lax.rsqrt(jnp.mean(t * t, axis=-1, keepdims=True) + EPS)
            return t * norm * scale
        b, t, _ = x.shape
        q = (x @ Wq.T).reshape(b, t, N_HEADS, HEAD_DIM).transpose(0, 2, 1, 3)
        k = (x @ Wk.T).reshape(b, t, N_KV_HEADS, HEAD_DIM).transpose(0, 2, 1, 3)
        v = (x @ Wv.T).reshape(b, t, N_KV_HEADS, HEAD_DIM).transpose(0, 2, 1, 3)
        q = _qknorm(q, q_scale)
        k = _qknorm(k, k_scale)
        k = jnp.repeat(k, N_REP, axis=1)
        v = jnp.repeat(v, N_REP, axis=1)
        scale = 1.0 / np.sqrt(HEAD_DIM).astype(np.float32)
        scores = jnp.einsum('bhtd,bhsd->bhts', q, k) * scale
        causal = jnp.tril(jnp.ones((t, t), dtype=bool))
        scores = jnp.where(causal, scores, jnp.finfo(scores.dtype).min)
        attn = jax.nn.softmax(scores, axis=-1)
        out = jnp.einsum('bhts,bhsd->bhtd', attn, v)
        out = out.transpose(0, 2, 1, 3).reshape(b, t, N_HEADS * HEAD_DIM)
        return out @ Wo.T

    def _L0_cond2_ref(r, k, v, w, u, time_emb):
        import jax, jax.numpy as jnp
        from jax import lax
        import numpy as np
        B, T, C, TD = (8, 256, 256, 64)

        def _bi_wkv(r, k, v, w, u, time_emb):
            tf = jax.nn.sigmoid(jnp.sum(time_emb, axis=-1))[:, None, None]
            decay = jnp.exp(-jnp.exp(w.astype(jnp.float32)))[None, :] * (0.5 + 0.5 * tf[:, :, 0])
            kf = k.astype(jnp.float32)
            vf = v.astype(jnp.float32)
            ek = jnp.exp(jnp.minimum(kf, 30.0))
            ekv = ek * vf

            def step(carry, x):
                a, b = carry
                ekv_t, ek_t = x
                a = a * decay + ekv_t
                b = b * decay + ek_t
                return ((a, b), (a, b))
            ekv_t = jnp.swapaxes(ekv, 0, 1)
            ek_t = jnp.swapaxes(ek, 0, 1)
            init = (jnp.zeros_like(decay), jnp.zeros_like(decay))
            _, (nf, df) = lax.scan(step, init, (ekv_t, ek_t))
            _, (nb, db) = lax.scan(step, init, (ekv_t, ek_t), reverse=True)
            nf = jnp.swapaxes(nf, 0, 1)
            df = jnp.swapaxes(df, 0, 1)
            nb = jnp.swapaxes(nb, 0, 1)
            db = jnp.swapaxes(db, 0, 1)
            euk = jnp.exp(jnp.minimum(u.astype(jnp.float32)[None, None, :] + kf, 30.0))
            num = nf + nb - ekv + euk * vf
            den = df + db - ek + euk
            base = jax.nn.sigmoid(r.astype(jnp.float32)) * (num / jnp.maximum(den, 1e-08))
            out = base * (0.8 + 0.2 * tf)
            return out.astype(r.dtype)
        return _bi_wkv(r, k, v, w, u, time_emb)

    def _L0_ffn_ref(hidden_states, gate_w, mask_up_w, gate_proj_w, up_proj_w, down_proj_w, inv_map):
        import jax, jax.numpy as jnp
        import numpy as np
        TOP_K = 8
        NEG_INF = -1000000000.0
        B, S, H = hidden_states.shape
        x = hidden_states.reshape(-1, H)
        N = x.shape[0]
        E = gate_w.shape[0]
        scores = jax.nn.softmax(x @ gate_w.T, axis=-1)
        topk_w, topk_idx = jax.lax.top_k(scores, TOP_K)
        w_e = jnp.zeros((N, E), x.dtype).at[jnp.arange(N)[:, None], topk_idx].add(topk_w)
        flat = w_e[:, inv_map]
        scalar = flat.sum(-1)
        soft = jax.nn.softmax(jnp.where(flat == 0, NEG_INF, flat), axis=-1)
        xg = x[:, None, :] + jnp.einsum('ngi,ghi->ngh', soft, mask_up_w)
        g = jnp.einsum('ngh,gih->ngi', xg, gate_proj_w)
        u = jnp.einsum('ngh,gih->ngi', xg, up_proj_w)
        a = jax.nn.silu(g) * u
        d = jnp.einsum('ngi,ghi->ngh', a, down_proj_w)
        y = jnp.einsum('ng,ngh->nh', scalar, d)
        return y.reshape(B, S, H)
    x = x + _L0_attn_ref(_L0_cond_ref(x, fside_BxSxS_0, fside_BxSxS_0, L0_cond_w, L0_cond_u, cond_512), L0_attn_Wq, L0_attn_Wk, L0_attn_Wv, L0_attn_Wo, L0_attn_q_scale, L0_attn_k_scale)
    x = x + _L0_ffn_ref(_L0_cond2_ref(x, fside_BxSxS_0, fside_BxSxS_0, L0_cond2_w, L0_cond2_u, cond_512), L0_ffn_gate_w, L0_ffn_mask_up_w, L0_ffn_gate_proj_w, L0_ffn_up_proj_w, L0_ffn_down_proj_w, L0_ffn_inv_map)
    return x

_drawn_inputs = setup_inputs


def setup_inputs(seed=0):
    import zlib

    import numpy as np

    out = dict(_drawn_inputs(seed))
    spreads = {'L0_attn_q_scale': (1.0, 0.6), 'L0_attn_k_scale': (1.0, 0.6)}
    factors = {'cond_512': 8.0,
     'L0_cond_u': 5.33,
     'L0_attn_Wq': 3.919,
     'L0_attn_Wk': 3.824,
     'L0_cond2_w': 8.0,
     'L0_cond2_u': 8.0,
     'L0_ffn_gate_w': 8.0,
     'L0_ffn_mask_up_w': 8.0,
     'L0_ffn_gate_proj_w': 8.0,
     'L0_ffn_up_proj_w': 8.0,
     'L0_ffn_down_proj_w': 8.0}
    for name, (base, spread) in spreads.items():
        noise = np.random.default_rng([zlib.crc32(name.encode()), seed]).standard_normal(out[name].shape)
        drawn = base * np.exp(spread * noise) if base else spread * noise
        out[name] = jnp.asarray(drawn.astype(out[name].dtype))
    for name, factor in factors.items():
        out[name] = (out[name] * factor).astype(out[name].dtype)
    return out
```

```python
from contextlib import ExitStack

import concourse.bass as bass
from concourse import mybir

ALU = mybir.AluOpType
ACT = mybir.ActivationFunctionType
F32 = mybir.dt.float32
F32R = mybir.dt.float32r
I32 = mybir.dt.int32
X = mybir.AxisListType.X

B, T, C = 4, 256, 256
NH, NKV, D = 16, 4, 128
REP = NH // NKV
G, GS, FI = 8, 8, 176
E = G * GS
TOPK = 8
P = 128
CH = C // P
NPAIR, PT_ = 2, 512
TPP = PT_ // P
FT = G * FI // P
EPS = 1e-6
NEG_BIG = -1.0e30
NSTAGE, NSLOT = 3, 5
KCAP = 30.0



ORDER = [("A", 0), ("D0", 3), ("L", 5), ("bg", 0), ("C", 1), ("D1", 3), ("N", 0), ("B", 0), ("X", 1), ("bg", 0),
         ("F", 5), ("S", 1), ("E", 4), ("rest", 0)]


def make_plan():
    plan = []

    def wkv(layer, b):
        return [("wkv", layer, b, k) for k in range(9)]

    def kv_k(p, half):
        t0 = 2 * half
        return [("K1", p, t0), ("K1", p, t0 + 1), ("K2", p, t0), ("K2", p, t0 + 1), ("K3", p, t0), ("K3", p, t0 + 1)]

    def kv_v(p, half):
        return [("V", p, 2 * half), ("V", p, 2 * half + 1)]

    first, second = wkv(1, 0), wkv(1, 1)
    plan += first[:3] + [("small",)] + first[3:6]
    plan += [("R", 0), ("R", 1), ("split", "K", 0)] + first[6:]
    plan += [("R", 2), ("R", 3), ("split", "Q", 0)] + second[:4]
    plan += kv_k(0, 0)
    bg = {i: [] for i in range(-1, 64)}
    bg[0] += second[4:]
    bg[0] += [("split", "V", 0)]
    bg[0] += [("R", 4), ("R", 5)]
    bg[1] += [("R", 6), ("R", 7)]
    for k, s in enumerate(wkv(1, 2)):
        bg[3 + k // 2].append(s)
    for k, s in enumerate(wkv(1, 3)):
        bg[8 + k // 2].append(s)
    for k, s in enumerate(wkv(2, 0)):
        bg[21 + k // 2].append(s)
    for k, s in enumerate(wkv(2, 1)):
        bg[26 + k // 2].append(s)
    for k in range(8):
        bg[min(31 + k, 37)].append(("route", 0, k))
    for p in range(NPAIR):
        for g in range(1, NKV):
            bg[16 * p + 4 * g - 3].append(("split", "Q", NKV * p + g))
        for g in range(NKV):
            bg[16 * p + 4 * g + 2].append(("split", "O", NKV * p + g))
    bg[13].append(("split", "K", 1))
    bg[14].append(("split", "Q", NKV))
    bg[17].append(("split", "V", 1))
    NI = 16 * NPAIR
    for i in range(NI + 6):
        p = i // 16
        todo = list(bg[i])
        if i in (1, 17):
            plan += kv_k(p, 1)
        if i == 15:
            late_k = kv_k(1, 0)
        else:
            late_k = []
        if i in (2, 18):
            plan += kv_v(p, 0)
        if i in (4, 20):
            plan += kv_v(p, 1)
        for kind, back in ORDER:
            m = i - back
            if kind == "bg":
                if todo:
                    plan.append(todo.pop(0))
            elif kind == "rest":
                plan += todo
                todo = []
            elif not 0 <= m < NI:
                continue
            elif kind == "D1":
                if m % 2:
                    plan.append(("D", m, 1))
            elif kind == "D0":
                plan.append(("D", m, 0))
            elif kind == "F":
                if m % 2:
                    plan.append(("F", m // 2))
                    if m % 16 == 15:
                        plan.append(("x1", m // 16))
            else:
                plan.append((kind, m))
        assert not todo
        plan += late_k
    last = wkv(2, 2) + wkv(2, 3) + [("route", 1, k) for k in range(8)]
    NF = FT * NPAIR
    plan += [("split", "F", 0), ("split", "F", 1), ("split", "F", 2)]
    per = {m: [] for m in range(NF)}
    for k, s in enumerate(last):
        per[k // 3].append(s)
    for f in range(NF + 2):
        if f < NF:
            plan.append(("G", f))
            if per[f]:
                plan.append(per[f].pop(0))
        if f >= 2:
            plan.append(("Y", f - 2))
            if (f - 2) % FT == FT - 1:
                plan.append(("out", (f - 2) // FT))
        if f + 3 < NF:
            plan.append(("split", "F", f + 3))
        if f < NF:
            plan += per[f]
    return plan


PLAN = make_plan()
BLOCKS = [s for s in PLAN if s[0] in ("R", "small", "split")]
BLOCK_NO = {s: n for n, s in enumerate(BLOCKS)}
SPLITS = [s for s in BLOCKS if s[0] in ("split", "small")]
SPLIT_NO = {s: n for n, s in enumerate(SPLITS)}
BLOCK_COLS = {"R": 4 * FI, "small": 256, "K": 1024, "V": 1024, "Q": 1024, "O": 1024, "F": 768}

PROJ_SPLITS = [s for s in SPLITS if s[0] == "split" and s[1] in "KVQ"]


def last_projection(s):
    if s[1] == "Q":
        return PROJ[("A", 4 * s[2] + 3)]
    return PROJ[("K1" if s[1] == "K" else "V", s[2], TPP - 1)]


def slot_of(s):
    if s[1] in "KVQ":
        return PROJ_SPLITS.index(s) % 3
    if s[1] == "O":
        return 3 + s[2] % 2
    return s[2] % NSLOT


def numbered(kinds):
    return {s: n for n, s in enumerate([s for s in PLAN if s[0] in kinds])}


TOK = numbered(("K1", "A"))
PROJ = {s: n for n, s in enumerate([s for s in PLAN if s[0] in ("K1", "A", "V", "R")
                                    or (s[0] == "route" and s[2] not in (2, 5))])}
PROJ_STEPS = list(PROJ)
WKV_CALL = {}
for _s in PLAN:
    if _s[0] == "wkv" and _s[1:3] not in WKV_CALL:
        WKV_CALL[_s[1:3]] = len(WKV_CALL)
TR_STEPS = [s for s in PLAN if s[0] in ("K3", "B", "D")]
TR = {s: n for n, s in enumerate(TR_STEPS)}
VNO = numbered(("V",))
RNO = numbered(("R",))
KNO = numbered(("K3",))
ROOT = numbered(("K2", "C"))
ND, NA, NPL = 22, 4, 3


def item(m):
    p, r = divmod(m, 16)
    g, t = divmod(r, 4)
    return p, g, t, t // 2, t % 2


def units_before(m):
    return m + m // 2


def unit_heads(ti, j):
    return range(REP) if ti == 0 else range(2 * j, 2 * j + 2)


unit_tr = {}
for _m in range(32):
    for _j in range(_m % 2 + 1):
        unit_tr[units_before(_m) + _j] = TR[("D", _m, _j)]


def program(nc, ins, out):
    ctx = ExitStack()
    with ctx:
        def sb(name, shape, dt=F32):
            return ctx.enter_context(nc.sbuf_tensor(name, shape, dt))

        def pb(name):
            return ctx.enter_context(nc.psum_tensor(name, [P, 512], F32))

        def sem(name):
            return ctx.enter_context(nc.semaphore(name))

        xT = sb("xT", [P, CH, B * T])
        fT = sb("fT", [P, CH, B * T])
        const = sb("const", [P, 128 + 256 + 1])
        ident, mask, iota = const[:, 0:128], const[:, 128:384], const[:, 384:385]
        vecs = sb("vecs", [P, 10])
        cond = sb("cond", [P, B, 64])
        imap = sb("imap", [E, E], I32)
        imapf = sb("imapf", [E, E])
        onehot = sb("onehot", [E, E])
        tf = sb("tf", [P, 4 * B])
        mix = sb("mix", [P, B])
        half = sb("half", [P, B])
        decay = sb("decay", [P, 2, CH, B])
        edec = sb("edec", [P, 8])
        qks = sb("qks", [P, 1])
        stage = sb("stage", [P, NSTAGE, 1024])
        WH = sb("WH", [P, NSLOT, 1024], F32R)
        WL = sb("WL", [P, NSLOT, 1024], F32R)
        GWH = sb("GWH", [P, CH, 128], F32R)
        GWL = sb("GWL", [P, CH, 128], F32R)
        IND = sb("IND", [64, FT * P], F32R)
        RH = sb("RH", [P, NPAIR, CH, PT_], F32R)
        RL = sb("RL", [P, NPAIR, CH, PT_], F32R)
        EK, EKV, EUK, EUF, NF, NB, DF, DB, SG = (sb(n, [P, CH, T]) for n in
                                                 ("EK", "EKV", "EUK", "EUF", "NF", "NB", "DF", "DB", "SG"))
        kT = sb("kT", [P, NKV, PT_])
        V = sb("V", [P, TPP, NKV * D])
        QS = sb("QS", [P, 2, REP * D])
        QT = sb("QT", [P, 2, REP, P])
        junk = sb("junk", [P, REP, D])
        NST = 8
        SS, VAR, LN, Y0, NA_, NB_, RQ = (sb(n, [P, NST, REP]) for n in ("SS", "VAR", "LN", "Y0", "NA_", "NB_", "RQ"))
        MX, NBI, RS, RI = (sb(n, [P, 4, REP]) for n in ("MX", "NBI", "RS", "RI"))
        PR = sb("PR", [P, 6, 512])
        PTS = sb("PTS", [P, 2, 2, REP, P])
        OH = sb("OH", [P, 1024], F32R)
        OL = sb("OL", [P, 1024], F32R)
        EXH = sb("EXH", [P, 2, FT * P], F32R)
        EXL = sb("EXL", [64, 2, FT * P], F32R)
        SX = sb("SX", [P, B * T], F32R)
        SCX = sb("SCX", [64, B * T], F32R)
        bmask = V[:, :, :].rearrange("p t n -> p (t n)").rearrange("p (c g d e) -> p c g d e", c=CH, g=G, d=2)
        mup = sb("mup", [P, CH, E])
        LT = EK[0:E, :, :].rearrange("p c n -> p (c n)")
        LG, SC, MR, FL = (x[:, h, :].rearrange("p (a n) -> p a n", a=TPP) for x in (EKV, EUK) for h in range(2))
        T8 = sb("T8", [P, TPP, 8])
        r4a, r4b, r4c = (sb(n, [P, TPP]) for n in ("r4a", "r4b", "r4c"))
        g8a, g8b = (sb(n, [P, TPP, G]) for n in ("g8a", "g8b"))
        ST = EUF[:, :, :].rearrange("p c n -> p (c n)").rearrange("p (a d e) -> p a d e", a=TPP, d=2)
        STS = sb("STS", [P, TPP, 64])
        OHs = OH[:, :].rearrange("p (h t) -> p h t", h=REP)
        OLs = OL[:, :].rearrange("p (h t) -> p h t", h=REP)

        acc = [pb("acc0"), pb("acc1")]
        proj = pb("proj")
        tr = [pb("tr0"), pb("tr1")]
        sc = [pb("sc0"), pb("sc1")]
        ov = pb("ov")

        names = """consts_in vecs_in cond_in side_in0 side_in1 side_in2 side_in3 x_in0 x_in1 x_in2 x_in3 ind_in mup_in imap_in stores_done
        init_act init_dve zeros_ready key_scale_ready bmask_ready onehot_ready indicator_ready
        split_hi split_lo ffn_used
        wkv_act wkv_dve wkv_pool
        proj_full tr_full tok_ready sumsq_done var_ready rs_act rq_ready kn_ready q_turned k_turned v_ready table_hi table_lo
        scores_full max_ready bias_ready exp_done rinv_ready p_ready pt_act pt_dve ov_full o_hi o_lo wo_done x1_ready
        gate_full up_full scal_full tanh_done gate_used up_used a_ready a_hi a_lo y_full result_ready
        rt_act rt_vec dve_link act_link pool_link""".split()
        s = {n: sem(n) for n in names}
        staged = [sem(f"staged{k}") for k in range(NSTAGE)]
        block = ctx.enter_context(nc.Block())

        def cols(b):
            return slice(b * T, (b + 1) * T)

        def wait_split(eng, step):
            eng.wait_ge(s["split_lo"], SPLIT_NO[step] + 1)

        def wait_r(eng, b, layer):
            eng.wait_ge(s["wkv_dve"], ND * (WKV_CALL[(layer, b)] + 1))

        def wait_proj_free(eng, step):
            n = PROJ[step]
            if n == 0:
                return
            q = PROJ_STEPS[n - 1]
            if q[0] in ("K1", "A"):
                eng.wait_ge(s["tok_ready"], TOK[q] + 1)
            elif q[0] == "V":
                eng.wait_ge(s["v_ready"], VNO[q] + 1)
            elif q[0] == "R":
                eng.wait_ge(s["table_lo"], RNO[q] + 1)
            elif q[2] in (0, 3):
                eng.wait_ge(s["rt_act"], RT_ACT[q[2]] + 6 * q[1])
            else:
                eng.wait_ge(s["rt_vec"], RT_VEC[q[2]] + 6 * q[1])

        RT_ACT = {0: 1, 2: 2, 3: 3, 5: 4, 6: 5, 7: 6}
        RT_VEC = {1: 1, 2: 2, 4: 3, 5: 4, 6: 5, 7: 6}

        def wait_turned(eng, t):
            q = TR_STEPS[t]
            if q[0] == "K3":
                eng.wait_ge(s["k_turned"], KNO[q] + 1)
            elif q[0] == "B":
                eng.wait_ge(s["q_turned"], q[1] + 1)
            elif q[2] == 0:
                eng.wait_ge(s["pt_act"], q[1] + 1)
            else:
                eng.wait_ge(s["pt_dve"], q[1] // 2 + 1)

        tok_tr = {}
        for q in TR_STEPS:
            if q[0] == "K3":
                tok_tr[TOK[("K1", q[1], q[2])]] = TR[q]
            elif q[0] == "B":
                tok_tr[TOK[("A", q[1])]] = TR[q]

        @block.sync
        def _(sp):
            sp.dma_start(vecs[:], ins["vecs"]).then_inc(s["vecs_in"], 16)
            sp.dma_start(cond[:], ins["cond"]).then_inc(s["cond_in"], 16)
            sp.dma_start(fT[:, :, cols(0)], ins["fT"][:, :, cols(0)]).then_inc(s["side_in0"], 16)
            sp.dma_start(xT[:, :, cols(0)], ins["xT"][:, :, cols(0)]).then_inc(s["x_in0"], 16)
            sp.dma_start(const[:], ins["const"]).then_inc(s["consts_in"], 16)
            sp.dma_start(mup[:], ins["mup"]).then_inc(s["mup_in"], 16)

            def load(n):
                step = BLOCKS[n]
                if n >= NSTAGE:
                    old = BLOCKS[n - NSTAGE]
                    if old[0] == "R":
                        sp.wait_ge(s["proj_full"], PROJ[old] + 1)
                    else:
                        sp.wait_ge(s["split_lo"], SPLIT_NO[old] + 1)
                w = BLOCK_COLS[step[1] if step[0] == "split" else step[0]]
                if step[0] == "R":
                    src = ins["tables"][step[1]]
                elif step[0] == "small":
                    src = ins["gate"]
                elif step[1] == "F":
                    src = ins["ffn"][step[2] % FT]
                else:
                    src = {"K": ins["wk"], "V": ins["wv"], "Q": ins["wq"][step[2] % NKV],
                           "O": ins["wo"][step[2] % NKV]}[step[1]]
                sp.dma_start(stage[:, n % NSTAGE, 0:w], src).then_inc(staged[n % NSTAGE], 16)

            for n in range(3):
                load(n)
            sp.dma_start(fT[:, :, cols(1)], ins["fT"][:, :, cols(1)]).then_inc(s["side_in1"], 16)
            sp.dma_start(xT[:, :, cols(1)], ins["xT"][:, :, cols(1)]).then_inc(s["x_in1"], 16)
            sp.dma_start(imap[:], ins["imap"]).then_inc(s["imap_in"], 16)
            for n in range(3, 8):
                load(n)
            sp.dma_start(fT[:, :, cols(2)], ins["fT"][:, :, cols(2)]).then_inc(s["side_in2"], 16)
            sp.dma_start(xT[:, :, cols(2)], ins["xT"][:, :, cols(2)]).then_inc(s["x_in2"], 16)
            sp.dma_start(fT[:, :, cols(3)], ins["fT"][:, :, cols(3)]).then_inc(s["side_in3"], 16)
            sp.dma_start(xT[:, :, cols(3)], ins["xT"][:, :, cols(3)]).then_inc(s["x_in3"], 16)
            sp.dma_start(PR[0:64, 0:3, :].rearrange("p a n -> p (a n)")[:, 0:FT * P], ins["ind"]).then_inc(s["ind_in"], 16)
            for n in range(8, len(BLOCKS)):
                load(n)
            for p in range(NPAIR):
                sp.wait_ge(s["result_ready"], 2 * (p + 1))
                tok = slice(p * PT_, (p + 1) * PT_)
                sp.dma_start(out[:, :, tok], xT[:, :, tok]).then_inc(s["stores_done"], 16)
            sp.wait_ge(s["stores_done"], 16 * NPAIR)

        @block.gpsimd
        def _(pool):
            link = [0]

            def linked(i):
                link[0] += 1
                i.then_inc(s["pool_link"], 1)
                pool.wait_ge(s["pool_link"], link[0])

            linked(pool.memset(V[:], 0.0))
            pool.memset(STS[:], 0.0).then_inc(s["zeros_ready"], 1)
            pool.wait_ge(s["mup_in"], 16)
            for g in range(G):
                for dup in range(2):
                    i = pool.tensor_copy(bmask[:, :, g, dup, GS * g:GS * g + GS], mup[:, :, GS * g:GS * g + GS])
                    if g == G - 1 and dup == 1:
                        i.then_inc(s["bmask_ready"], 1)
            for st in PLAN:
                if st[0] == "small" or st[0] == "split":
                    n, blk = SPLIT_NO[st], BLOCK_NO[st]
                    src = stage[:, blk % NSTAGE, :]
                    pool.wait_ge(staged[blk % NSTAGE], 16 * (blk // NSTAGE + 1))
                    pool.wait_ge(s["split_hi"], n + 1)
                    if st[0] == "small":
                        w = CH * P
                        hi, lo = (x[:, :, :].rearrange("p c n -> p (c n)") for x in (GWH, GWL))
                    else:
                        w = BLOCK_COLS[st[1]]
                        hi, lo = WH[:, slot_of(st), 0:w], WL[:, slot_of(st), 0:w]
                    pool.tensor_tensor(lo, src[:, 0:w], hi.bitcast(F32), ALU.subtract).then_inc(s["split_lo"], 1)
                elif st[0] == "wkv":
                    _, L, b, k = st
                    w = WKV_CALL[(L, b)]
                    f = fT[:, :, cols(b)]
                    if k == 2:
                        pool.wait_ge(s["wkv_act"], NA * w + 2)
                        if w:
                            pool.wait_ge(s["wkv_dve"], ND * w)
                        pool.wait_ge(s[f"side_in{b}"], 16)
                        pool.tensor_tensor(EUF[:], EUK[:], f, ALU.mult).then_inc(s["wkv_pool"], 1)
                    if k == 3:
                        pool.wait_ge(s["wkv_pool"], NPL * w + 1)
                        pool.wait_ge(s["wkv_dve"], ND * w + 4)
                        pool.tensor_tensor(EUF[:], EUF[:], EKV[:], ALU.subtract).then_inc(s["wkv_pool"], 1)
                        pool.tensor_tensor(EUK[:], EUK[:], EK[:], ALU.subtract).then_inc(s["wkv_pool"], 1)
                elif st[0] == "S":
                    m = st[1]
                    p, g, t, bb, ti = item(m)
                    for j in range(ti + 1):
                        u = units_before(m) + j
                        hs = unit_heads(ti, j)
                        nh = len(hs)
                        pr = PR[:, u % 6, :].rearrange("p (h n) -> p h n", h=nh)
                        pool.wait_ge(s["rinv_ready"], u + 1)
                        pool.tensor_tensor(pr, pr, RI[:, m % 4, hs[0]:hs[0] + nh].rearrange("p (h o) -> p h o", o=1).broadcast_to([P, nh, 512 // nh]),
                                           ALU.mult).then_inc(s["p_ready"], 1)
                elif st[0] == "G":
                    f = st[1]
                    sl = slice(512 * (f % 2), 512 * (f % 2) + 512)
                    pool.wait_ge(s["a_hi"], f + 1)
                    pool.tensor_tensor(OL[:, sl], PR[:, 4 + f % 2, :], OH[:, sl].bitcast(F32),
                                       ALU.subtract).then_inc(s["a_lo"], 1)

        @block.scalar
        def _(act):
            def exp(o, i, **k):
                return nc.scalar.activation(o, i, ACT.Exp, **k)

            nc.scalar.preload_act_table_set("natural_log_exp_and_others")
            act.wait_ge(s["init_dve"], 1)
            exp(tf[:, B:2 * B], tf[:, 0:B], scale=-1.0).then_inc(s["init_act"], 1)
            act.wait_ge(s["vecs_in"], 16)
            exp(edec[:], vecs[:, 0:8]).then_inc(s["init_act"], 1)
            act.wait_ge(s["init_act"], 2)
            exp(edec[:, :], edec[:, :], scale=-1.0).then_inc(s["init_act"], 1)

            for st in PLAN:
                if st[0] in ("small", "split"):
                    n, blk = SPLIT_NO[st], BLOCK_NO[st]
                    act.wait_ge(staged[blk % NSTAGE], 16 * (blk // NSTAGE + 1))
                    src = stage[:, blk % NSTAGE, :]
                    if st[0] == "small":
                        nc.scalar.copy(GWH[:, :, :].rearrange("p c n -> p (c n)"), src[:, 0:256]).then_inc(s["split_hi"], 1)
                        continue
                    w, slot = BLOCK_COLS[st[1]], slot_of(st)
                    old = None
                    if st[1] in "KVQ":
                        k = PROJ_SPLITS.index(st)
                        old = PROJ_SPLITS[k - 3] if k >= 3 else None
                    elif st[1] == "O":
                        if st[2] >= 2:
                            act.wait_ge(s["wo_done"], 2 * (st[2] - 1))
                    elif st[2] < 3:
                        old = [q for q in PROJ_SPLITS if slot_of(q) == slot][-1]
                    elif st[2] < NSLOT:
                        act.wait_ge(s["wo_done"], 16)
                    else:
                        act.wait_ge(s["ffn_used"], st[2] - 4)
                    if old:
                        act.wait_ge(s["proj_full"], last_projection(old) + 1)
                    nc.scalar.copy(WH[:, slot, 0:w], src[:, 0:w]).then_inc(s["split_hi"], 1)
                elif st[0] == "wkv":
                    _, L, b, k = st
                    w = WKV_CALL[(L, b)]
                    if k == 1:
                        act.wait_ge(s["wkv_dve"], ND * w + 1)
                        exp(EK[:], EK[:]).then_inc(s["wkv_act"], 1)
                        act.wait_ge(s["wkv_dve"], ND * w + 3)
                        exp(EUK[:], EUK[:]).then_inc(s["wkv_act"], 1)
                        if L == 1:
                            act.wait_ge(s[f"x_in{b}"], 16)
                        else:
                            act.wait_ge(s["x1_ready"], 2 * (b // 2 + 1))
                        exp(SG[:], xT[:, :, cols(b)], scale=-1.0).then_inc(s["wkv_act"], 1)
                    if k == 7:
                        act.wait_ge(s["wkv_dve"], ND * w + 21)
                        if L == 2:
                            last = max(PROJ[q] for q in PROJ if q[0] == "V" and q[1] == b // 2)
                            last = max(last, PROJ[("A", 16 * (b // 2) + 15)])
                            act.wait_ge(s["proj_full"], last + 1)
                        nc.scalar.copy(RH[:, b // 2, :, cols(b % 2)], NF[:]).then_inc(s["wkv_act"], 1)
                elif st[0] in ("K1", "A"):
                    e = TOK[st]
                    act.wait_ge(s["proj_full"], PROJ[st] + 1)
                    if e >= 2:
                        act.wait_ge(s["tr_full"], tok_tr[e - 2] + 1)
                        act.wait_ge(s["sumsq_done"], e - 1)
                    nc.scalar.copy(QS[:, e % 2, :], proj[:]).then_inc(s["tok_ready"], 1)
                elif st[0] in ("N", "K2"):
                    e = TOK[("A", st[1]) if st[0] == "N" else ("K1", st[1], st[2])]
                    act.wait_ge(s["var_ready"], e + 1)
                    nc.scalar.activation(LN[:, e % NST, :], VAR[:, e % NST, :], ACT.Ln).then_inc(s["act_link"], 1)
                    act.wait_ge(s["act_link"], e + 1)
                    exp(Y0[:, e % NST, :], LN[:, e % NST, :], scale=-0.5).then_inc(s["rs_act"], 1)
                elif st[0] == "K3":
                    t = TR[st]
                    act.wait_ge(s["tr_full"], t + 1)
                    act.wait_ge(s["key_scale_ready"], 1)
                    if st[1] == 1:
                        act.wait_ge(s["scores_full"], units_before(13 + (2 if st[2] >= 2 else 0)) + 2)
                    nc.scalar.activation(kT[:, :, P * st[2]:P * st[2] + P], tr[t % 2][:].rearrange("p (g n) -> p g n", g=NKV),
                                         ACT.Copy, scale=qks[:, 0:1]).then_inc(s["k_turned"], 1)
                elif st[0] == "V":
                    act.wait_ge(s["proj_full"], PROJ[st] + 1)
                    if st[1] == 1:
                        act.wait_ge(s["ov_full"], 14 + (2 if st[2] >= 2 else 0))
                    nc.scalar.copy(V[:, st[2], :], proj[:]).then_inc(s["v_ready"], 1)
                elif st[0] == "R":
                    g = st[1]
                    act.wait_ge(s["proj_full"], PROJ[st] + 1)
                    nc.scalar.copy(EXH[:, :, g * FI:(g + 1) * FI], proj[:, 0:2 * FI].rearrange("p (a n) -> p a n", a=2)).then_inc(s["table_hi"], 1)
                elif st[0] == "B":
                    m, t = st[1], TR[st]
                    act.wait_ge(s["tr_full"], t + 1)
                    if m >= 2:
                        act.wait_ge(s["scores_full"], units_before(m - 1))
                    nc.scalar.copy(QT[:, m % 2, :, :], tr[t % 2][:].rearrange("p (h n) -> p h n", h=REP)).then_inc(s["q_turned"], 1)
                elif st[0] == "X":
                    m = st[1]
                    p, g, t, bb, ti = item(m)
                    e = TOK[("A", m)]
                    for j in range(ti + 1):
                        u = units_before(m) + j
                        hs = unit_heads(ti, j)
                        w = 512 // len(hs)
                        act.wait_ge(s["bias_ready"], u + 1)
                        for k, h in enumerate(hs):
                            i = exp(PR[:, u % 6, w * k:w * k + w], PR[:, u % 6, w * k:w * k + w], bias=NBI[:, m % 4, h:h + 1],
                                    scale=RQ[:, e % NST, h:h + 1], accum_out=RS[:, m % 4, h:h + 1])
                        i.then_inc(s["exp_done"], 1)
                elif st[0] == "D" and st[2] == 0:
                    m, t = st[1], TR[st]
                    ti = item(m)[4]
                    act.wait_ge(s["tr_full"], t + 1)
                    if m >= 2:
                        act.wait_ge(s["ov_full"], m - 1)
                    if ti == 0:
                        o, i = PTS[:, m % 2, 0, :, :].rearrange("p h n -> p (h n)"), tr[t % 2][:]
                    else:
                        o = PTS[:, m % 2, :, 0:2, :].rearrange("p s h n -> p s (h n)")
                        i = tr[t % 2][:].rearrange("p (s n) -> p s n", s=2)
                    nc.scalar.copy(o, i).then_inc(s["pt_act"], 1)
                elif st[0] == "E":
                    m = st[1]
                    ti = item(m)[4]
                    act.wait_ge(s["ov_full"], m + 1)
                    if m >= 2:
                        act.wait_ge(s["wo_done"], m // 2)
                    nc.scalar.copy(OHs[:, :, P * ti:P * ti + P], ov[:].rearrange("p (h n) -> p h n", h=REP)).then_inc(s["o_hi"], 1)
                elif st[0] == "route":
                    _, p, k = st
                    tok = slice(p * PT_, (p + 1) * PT_)
                    if k in (0, 3, 6, 7):
                        act.wait_ge(s["proj_full"], PROJ[st] + 1)
                    if k in (0, 3):
                        if k == 0 and p:
                            act.wait_ge(s["proj_full"], PROJ[("route", 0, 7)] + 1)
                        nc.scalar.copy(LT, proj[0:E, :]).then_inc(s["rt_act"], 1)
                    if k == 2:
                        act.wait_ge(s["rt_vec"], 6 * p + RT_VEC[1])
                        exp(LG, LG).then_inc(s["rt_act"], 1)
                    if k == 5:
                        act.wait_ge(s["rt_vec"], 6 * p + RT_VEC[4])
                        exp(MR, MR).then_inc(s["rt_act"], 1)
                    if k == 6:
                        nc.scalar.copy(SX[:, tok], proj[:]).then_inc(s["rt_act"], 1)
                    if k == 7:
                        nc.scalar.copy(SCX[:, tok], proj[0:64, :]).then_inc(s["rt_act"], 1)
                elif st[0] == "G":
                    f = st[1]
                    act.wait_ge(s["gate_full"], f + 1)
                    if f >= 2:
                        act.wait_ge(s["gate_used"], f - 1)
                    else:
                        act.wait_ge(s["tr_full"], len(TR_STEPS))
                    nc.scalar.activation(PR[:, f % 2, :], sc[f % 2][:], ACT.Tanh, scale=0.5).then_inc(s["tanh_done"], 1)
                    act.wait_ge(s["a_ready"], f + 1)
                    if f >= 2:
                        act.wait_ge(s["ffn_used"], f - 1)
                    else:
                        act.wait_ge(s["wo_done"], 16)
                    nc.scalar.copy(OH[:, 512 * (f % 2):512 * (f % 2) + 512], PR[:, 4 + f % 2, :]).then_inc(s["a_hi"], 1)
                if st == ("wkv", 1, 1, 8):
                    act.wait_ge(s["ind_in"], 16)
                    nc.scalar.copy(IND[:], PR[0:64, 0:3, :].rearrange("p a n -> p (a n)")[:, 0:FT * P]).then_inc(s["indicator_ready"], 1)

        @block.vector
        def _(dve):
            v = nc.vector
            link = [0]

            def linked(i):
                link[0] += 1
                i.then_inc(s["dve_link"], 1)
                dve.wait_ge(s["dve_link"], link[0])

            dve.wait_ge(s["cond_in"], 16)
            v.tensor_reduce(tf[:, 0:B], cond[:], X, ALU.add).then_inc(s["init_dve"], 1)
            dve.wait_ge(s["vecs_in"], 16)
            v.tensor_scalar(qks[:], vecs[:, 8:9], vecs[:, 9:10], float(D) ** -0.5, ALU.mult, ALU.mult).then_inc(s["key_scale_ready"], 1)
            dve.wait_ge(s["init_act"], 1)
            linked(v.tensor_scalar(tf[:, 2 * B:3 * B], tf[:, B:2 * B], 1.0, None, ALU.add))
            linked(v.reciprocal(tf[:, 3 * B:4 * B], tf[:, 2 * B:3 * B]))
            linked(v.tensor_scalar(mix[:], tf[:, 3 * B:4 * B], 0.2, 0.8, ALU.mult, ALU.add))
            linked(v.tensor_scalar(half[:], tf[:, 3 * B:4 * B], 0.5, 0.5, ALU.mult, ALU.add))
            dve.wait_ge(s["init_act"], 3)
            for L in range(2):
                for ch in range(CH):
                    linked(v.tensor_scalar(decay[:, L, ch, :], half[:], edec[:, 4 * L + ch:4 * L + ch + 1], None, ALU.mult))

            def wkv(L, b, k):
                w = WKV_CALL[(L, b)]
                f = fT[:, :, cols(b)]
                n0 = ND * w

                def done(i):
                    i.then_inc(s["wkv_dve"], 1)

                def after(n):
                    dve.wait_ge(s["wkv_dve"], n0 + n)

                if k == 0:
                    dve.wait_ge(s[f"side_in{b}"], 16)
                    if w:
                        dve.wait_ge(s["wkv_dve"], n0)
                        dve.wait_ge(s["wkv_pool"], NPL * w)
                    if (L, b) == (2, 2):
                        dve.wait_ge(s["proj_full"], PROJ[("route", 0, 7)] + 1)
                    done(v.tensor_scalar(EK[:], f, KCAP, None, ALU.min))
                    for ch in range(CH):
                        done(v.tensor_scalar(EUK[:, ch, :], f[:, ch, :], vecs[:, 4 * (L - 1) + 2 + ch:4 * (L - 1) + 3 + ch], KCAP,
                                             ALU.add, ALU.min))
                elif k == 2:
                    dve.wait_ge(s["wkv_act"], NA * w + 1)
                    done(v.tensor_tensor(EKV[:], EK[:], f, ALU.mult))
                elif k in (3, 4):
                    after(4)
                    ch = k - 3
                    d = decay[:, L - 1, ch, b:b + 1].broadcast_to([P, T])
                    done(v.tensor_tensor_scan(NF[:, ch, :], d, EKV[:, ch, :], 0.0, ALU.mult, ALU.add))
                    done(v.tensor_tensor_scan(DF[:, ch, :], d, EK[:, ch, :], 0.0, ALU.mult, ALU.add))
                    done(v.tensor_tensor_scan(NB[:, ch, ::-1], d, EKV[:, ch, ::-1], 0.0, ALU.mult, ALU.add))
                    done(v.tensor_tensor_scan(DB[:, ch, ::-1], d, EK[:, ch, ::-1], 0.0, ALU.mult, ALU.add))
                elif k == 5:
                    after(12)
                    done(v.tensor_tensor(NF[:], NF[:], NB[:], ALU.add))
                    done(v.tensor_tensor(DF[:], DF[:], DB[:], ALU.add))
                    dve.wait_ge(s["wkv_pool"], NPL * w + 3)
                    after(13)
                    done(v.tensor_tensor(NF[:], NF[:], EUF[:], ALU.add))
                    after(14)
                    done(v.tensor_tensor(DF[:], DF[:], EUK[:], ALU.add))
                    after(16)
                    done(v.tensor_scalar(DF[:], DF[:], 1e-8, None, ALU.max))
                    dve.wait_ge(s["wkv_act"], NA * w + 3)
                    after(17)
                    done(v.scalar_tensor_tensor(out=DF[:], in0=SG[:], scalar=1.0, in1=DF[:], op0=ALU.add, op1=ALU.mult))
                elif k == 6:
                    after(18)
                    done(v.reciprocal(DF[:, 0, :], DF[:, 0, :]))
                    done(v.reciprocal(DF[:, 1, :], DF[:, 1, :]))
                    after(20)
                    done(v.scalar_tensor_tensor(out=NF[:], in0=NF[:], scalar=mix[:, b:b + 1], in1=DF[:], op0=ALU.mult, op1=ALU.mult))
                elif k == 8:
                    dve.wait_ge(s["wkv_act"], NA * w + 4)
                    hi = RH[:, b // 2, :, cols(b % 2)]
                    done(v.tensor_tensor(RL[:, b // 2, :, cols(b % 2)], NF[:], hi.bitcast(F32), ALU.subtract))

            def sum_squares(st):
                e = TOK[st]
                dve.wait_ge(s["tok_ready"], e + 1)
                if e:
                    dve.wait_ge(s["sumsq_done"], e)
                if e >= NST:
                    dve.wait_ge(s["rs_act"], e - NST + 1)
                for h in range(REP):
                    q = QS[:, e % 2, D * h:D * h + D]
                    i = v.tensor_tensor_reduce(junk[:, h, :], q, q, 1.0, 0.0, ALU.mult, ALU.add, SS[:, e % NST, h:h + 1])
                i.then_inc(s["sumsq_done"], 1)
                dve.wait_ge(s["sumsq_done"], e + 1)
                v.tensor_scalar(VAR[:, e % NST, :], SS[:, e % NST, :], 1.0 / D, EPS, ALU.mult, ALU.add).then_inc(s["var_ready"], 1)

            def refine(st):
                e = TOK[st]
                dve.wait_ge(s["rs_act"], e + 1)
                y, a, b_, r, var = (x[:, e % NST, :] for x in (Y0, NA_, NB_, RQ, VAR))
                linked(v.scalar_tensor_tensor(out=a, in0=y, scalar=-0.5, in1=var, op0=ALU.mult, op1=ALU.mult))
                linked(v.tensor_tensor(b_, a, y, ALU.mult))
                v.scalar_tensor_tensor(out=r, in0=b_, scalar=1.5, in1=y, op0=ALU.add, op1=ALU.mult).then_inc(s["rq_ready"], 1)

            def route(p, k):
                tok = slice(p * PT_, (p + 1) * PT_)

                def last(i):
                    i.then_inc(s["rt_vec"], 1)

                def spread(x, n):
                    return x.rearrange("p a (b o) -> p a b o", o=1).broadcast_to([P, TPP, G, n])

                def spread3(x):
                    return x.rearrange("p (a o) -> p a o", o=1).broadcast_to([P, TPP, E])

                pj = proj[:, 0:TPP * E].rearrange("p (a n) -> p a n", a=TPP)
                if k == 1:
                    dve.wait_ge(s["proj_full"], PROJ[("route", p, 1)] + 1)
                    linked(v.tensor_reduce(r4a[:], pj, X, ALU.max))
                    last(v.tensor_tensor(LG, pj, spread3(r4a[:]), ALU.subtract))
                elif k == 2:
                    dve.wait_ge(s["rt_act"], 6 * p + 2)
                    linked(v.tensor_reduce(r4b[:], LG, X, ALU.add))
                    linked(v.reciprocal(r4c[:], r4b[:]))
                    linked(v.tensor_tensor(SC, LG, spread3(r4c[:]), ALU.mult))
                    for t in range(TPP):
                        v.max(T8[:, t, :], SC[:, t, :]).then_inc(s["dve_link"], 1)
                    link[0] += TPP
                    dve.wait_ge(s["dve_link"], link[0])
                    for t in range(TPP):
                        v.match_replace(MR[:, t, :], T8[:, t, :], SC[:, t, :], 0.0).then_inc(s["dve_link"], 1)
                    link[0] += TPP
                    dve.wait_ge(s["dve_link"], link[0])
                    last(v.tensor_tensor(SC, SC, MR, ALU.subtract))
                elif k == 4:
                    dve.wait_ge(s["proj_full"], PROJ[("route", p, 4)] + 1)
                    linked(v.tensor_copy(FL, pj))
                    linked(v.tensor_reduce(g8a[:], FL.rearrange("p a (g j) -> p a g j", g=G), X, ALU.add))
                    linked(v.tensor_copy(STS[:, :, 0:G], g8a[:]))
                    linked(v.tensor_copy(STS[:, :, 32:32 + G], g8a[:]))
                    linked(v.tensor_scalar(MR, FL, 0.0, -1e9, ALU.is_equal, ALU.mult))
                    linked(v.tensor_tensor(MR, MR, FL, ALU.add))
                    m4 = MR.rearrange("p a (g j) -> p a g j", g=G)
                    linked(v.tensor_reduce(g8b[:], m4, X, ALU.max))
                    last(v.tensor_tensor(m4, m4, spread(g8b[:], GS), ALU.subtract))
                elif k == 5:
                    dve.wait_ge(s["rt_act"], 6 * p + 4)
                    m4 = MR.rearrange("p a (g j) -> p a g j", g=G)
                    linked(v.tensor_reduce(g8a[:], m4, X, ALU.add))
                    linked(v.reciprocal(g8b[:], g8a[:]))
                    linked(v.tensor_tensor(FL.rearrange("p a (g j) -> p a g j", g=G), m4, spread(g8b[:], GS), ALU.mult))
                    linked(v.tensor_copy(ST[:, :, 0, :], FL))
                    last(v.tensor_copy(ST[:, :, 1, :], FL))
                elif k == 6:
                    dve.wait_ge(s["rt_act"], 6 * p + 5)
                    last(v.tensor_tensor(SX[64:128, tok], proj[64:128, :], SX[64:128, tok].bitcast(F32), ALU.subtract))
                elif k == 7:
                    dve.wait_ge(s["rt_act"], 6 * p + 6)
                    last(v.tensor_tensor(SCX[32:64, tok], proj[32:64, :], SCX[32:64, tok].bitcast(F32), ALU.subtract))

            for st in PLAN:
                if st[0] == "wkv":
                    wkv(*st[1:])
                elif st[0] in ("K1", "A"):
                    sum_squares(st)
                elif st[0] == "K2":
                    q = ("K1", st[1], st[2])
                    e = TOK[q]
                    refine(q)
                    dve.wait_ge(s["rq_ready"], ROOT[st] + 1)
                    qs = QS[:, e % 2, :].rearrange("p (h n) -> p h n", h=REP)
                    v.tensor_tensor(qs, qs, RQ[:, e % NST, :].rearrange("p (h o) -> p h o", o=1).broadcast_to([P, REP, D]),
                                    ALU.mult).then_inc(s["kn_ready"], 1)
                elif st[0] == "R":
                    g = st[1]
                    dve.wait_ge(s["table_hi"], RNO[st] + 1)
                    v.tensor_tensor(EXL[:, :, g * FI:(g + 1) * FI], proj[0:64, 0:2 * FI].rearrange("p (a n) -> p a n", a=2),
                                    EXH[0:64, :, g * FI:(g + 1) * FI].bitcast(F32), ALU.subtract).then_inc(s["table_lo"], 1)
                elif st[0] == "C":
                    m = st[1]
                    p, g, t, bb, ti = item(m)
                    e = TOK[("A", m)]
                    refine(("A", m))
                    for j in range(ti + 1):
                        u = units_before(m) + j
                        hs = unit_heads(ti, j)
                        nh, w = len(hs), 512 // len(hs)
                        dve.wait_ge(s["scores_full"], u + 1)
                        if u >= 6:
                            q = unit_tr[u - 6]
                            dve.wait_ge(s["tr_full"], q + 1)
                        if u == 0:
                            dve.wait_ge(s["indicator_ready"], 1)
                        for k, h in enumerate(hs):
                            i = v.tensor_tensor_reduce(PR[:, u % 6, w * k:w * k + w], sc[u % 2][:, w * k:w * k + w],
                                                       mask[:, 256 - w:256], 1.0, NEG_BIG, ALU.add, ALU.max, MX[:, m % 4, h:h + 1])
                        i.then_inc(s["max_ready"], 1)
                        dve.wait_ge(s["max_ready"], u + 1)
                        dve.wait_ge(s["rq_ready"], ROOT[st] + 1)
                        v.scalar_tensor_tensor(out=NBI[:, m % 4, hs[0]:hs[0] + nh], in0=MX[:, m % 4, hs[0]:hs[0] + nh], scalar=-1.0,
                                               in1=RQ[:, e % NST, hs[0]:hs[0] + nh], op0=ALU.mult, op1=ALU.mult).then_inc(s["bias_ready"], 1)
                elif st[0] == "S":
                    m = st[1]
                    ti = item(m)[4]
                    for j in range(ti + 1):
                        u = units_before(m) + j
                        hs = unit_heads(ti, j)
                        dve.wait_ge(s["exp_done"], u + 1)
                        v.reciprocal(RI[:, m % 4, hs[0]:hs[0] + len(hs)], RS[:, m % 4, hs[0]:hs[0] + len(hs)]).then_inc(s["rinv_ready"], 1)
                elif st[0] == "D" and st[2] == 1:
                    m, t = st[1], TR[st]
                    dve.wait_ge(s["tr_full"], t + 1)
                    if m >= 2:
                        dve.wait_ge(s["ov_full"], m - 1)
                    v.tensor_copy(PTS[:, m % 2, :, 2:4, :].rearrange("p s h n -> p s (h n)"),
                                  tr[t % 2][:].rearrange("p (s n) -> p s n", s=2)).then_inc(s["pt_dve"], 1)
                elif st[0] == "L":
                    m = st[1]
                    ti = item(m)[4]
                    dve.wait_ge(s["o_hi"], m + 1)
                    v.tensor_tensor(OLs[:, :, P * ti:P * ti + P], ov[:].rearrange("p (h n) -> p h n", h=REP),
                                    OHs[:, :, P * ti:P * ti + P].bitcast(F32), ALU.subtract).then_inc(s["o_lo"], 1)
                elif st[0] == "x1":
                    p = st[1]
                    dve.wait_ge(s["wo_done"], 8 * (p + 1))
                    for mc in range(2):
                        o = xT[:, mc, p * PT_:(p + 1) * PT_]
                        v.tensor_tensor(o, o, acc[mc][:], ALU.add).then_inc(s["x1_ready"], 1)
                elif st[0] == "route":
                    route(st[1], st[2])
                elif st[0] == "G":
                    f = st[1]
                    dve.wait_ge(s["tanh_done"], f + 1)
                    if f >= 2:
                        dve.wait_ge(s["up_used"], f - 1)
                    v.scalar_tensor_tensor(out=PR[:, 2 + f % 2, :], in0=PR[:, f % 2, :], scalar=1.0, in1=sc[f % 2][:],
                                           op0=ALU.add, op1=ALU.mult).then_inc(s["gate_used"], 1)
                    dve.wait_ge(s["up_full"], f + 1)
                    dve.wait_ge(s["gate_used"], f + 1)
                    v.tensor_tensor(PR[:, 2 + f % 2, :], PR[:, 2 + f % 2, :], tr[f % 2][:], ALU.mult).then_inc(s["up_used"], 1)
                    dve.wait_ge(s["scal_full"], f + 1)
                    dve.wait_ge(s["up_used"], f + 1)
                    if f >= 2:
                        dve.wait_ge(s["a_lo"], f - 1)
                    v.scalar_tensor_tensor(out=PR[:, 4 + f % 2, :], in0=PR[:, 2 + f % 2, :], scalar=0.5, in1=ov[:],
                                           op0=ALU.mult, op1=ALU.mult).then_inc(s["a_ready"], 1)
                elif st[0] == "out":
                    p = st[1]
                    dve.wait_ge(s["ffn_used"], FT * (p + 1))
                    for mc in range(2):
                        o = xT[:, mc, p * PT_:(p + 1) * PT_]
                        v.tensor_tensor(o, o, acc[mc][:], ALU.add).then_inc(s["result_ready"], 1)
                if st == ("wkv", 1, 1, 8):
                    dve.wait_ge(s["imap_in"], 16)
                    linked(v.tensor_copy(imapf[:], imap[:]))
                    dve.wait_ge(s["consts_in"], 16)
                    v.tensor_scalar(onehot[:], imapf[:], iota[0:E, :], None, ALU.is_equal).then_inc(s["onehot_ready"], 1)

        @block.tensor
        def _(pe):
            mm, tp = nc.tensor.matmul, nc.tensor.transpose

            def three(o, lh, ll, rh, rl, first, last):
                mm(o, lh, rh, start=first, stop=False, skip_group_check=True)
                mm(o, lh, rl, start=False, stop=False, skip_group_check=True)
                return mm(o, ll, rh, start=False, stop=last, skip_group_check=True)

            def wblock(st, lo, hi):
                return WH[:, slot_of(st), lo:hi], WL[:, slot_of(st), lo:hi]

            def project(st, p, t, wst):
                wait_split(pe, wst)
                wait_r(pe, 2 * p + t // 2, 1)
                wait_proj_free(pe, st)
                for ch in range(CH):
                    a = [x[:, p, ch, P * t:P * t + P] for x in (RH, RL)]
                    w = wblock(wst, 512 * ch, 512 * ch + 512)
                    i = three(proj[:], a[0], a[1], w[0], w[1], ch == 0, ch == CH - 1)
                i.then_inc(s["proj_full"], 1)

            def turn(st, blocks):
                t = TR[st]
                if t >= 2:
                    wait_turned(pe, t - 2)
                for k, x in enumerate(blocks):
                    i = tp(tr[t % 2][:, P * k:P * k + P], x, ident)
                i.then_inc(s["tr_full"], 1)

            pe.wait_ge(s["consts_in"], 16)
            for st in PLAN:
                if st[0] == "R":
                    g, blk = st[1], BLOCK_NO[st]
                    pe.wait_ge(staged[blk % NSTAGE], 16 * (blk // NSTAGE + 1))
                    if RNO[st] == 0:
                        pe.wait_ge(s["bmask_ready"], 1)
                    wait_proj_free(pe, st)
                    wts = stage[:, blk % NSTAGE, 0:4 * FI].rearrange("p (a c n) -> p a c n", a=2, c=CH)
                    for a in range(2):
                        for ch in range(CH):
                            i = mm(proj[:, a * FI:(a + 1) * FI], bmask[:, ch, g, :, :].rearrange("p d e -> p (d e)"), wts[:, a, ch, :],
                                   start=(ch == 0), stop=(ch == CH - 1))
                    i.then_inc(s["proj_full"], 1)
                elif st[0] == "K1":
                    project(st, st[1], st[2], ("split", "K", st[1]))
                elif st[0] == "V":
                    project(st, st[1], st[2], ("split", "V", st[1]))
                elif st[0] == "A":
                    p, g, t, bb, ti = item(st[1])
                    project(st, p, t, ("split", "Q", NKV * p + g))
                elif st[0] == "K3":
                    e = TOK[("K1", st[1], st[2])]
                    pe.wait_ge(s["kn_ready"], KNO[st] + 1)
                    turn(st, [QS[:, e % 2, D * h:D * h + D] for h in range(NKV)])
                elif st[0] == "B":
                    e = TOK[("A", st[1])]
                    pe.wait_ge(s["tok_ready"], e + 1)
                    turn(st, [QS[:, e % 2, D * h:D * h + D] for h in range(REP)])
                elif st[0] == "C":
                    m = st[1]
                    p, g, t, bb, ti = item(m)
                    pe.wait_ge(s["q_turned"], m + 1)
                    pe.wait_ge(s["k_turned"], 4 * p + t + 1)
                    for j in range(ti + 1):
                        u = units_before(m) + j
                        hs = unit_heads(ti, j)
                        w = 512 // len(hs)
                        if u >= 2:
                            pe.wait_ge(s["max_ready"], u - 1)
                        for k, h in enumerate(hs):
                            i = mm(sc[u % 2][:, w * k:w * k + w], QT[:, m % 2, h, :], kT[:, g, T * bb:T * bb + w], start=True, stop=True)
                        i.then_inc(s["scores_full"], 1)
                elif st[0] == "D":
                    m, j = st[1], st[2]
                    ti = item(m)[4]
                    u = units_before(m) + j
                    pe.wait_ge(s["p_ready"], u + 1)
                    pr = PR[:, u % 6, :]
                    if ti == 0:
                        turn(st, [pr[:, P * h:P * h + P] for h in range(REP)])
                    else:
                        turn(st, [pr[:, T * h + P * c:T * h + P * c + P] for c in range(2) for h in range(2)])
                elif st[0] == "E":
                    m = st[1]
                    p, g, t, bb, ti = item(m)
                    pe.wait_ge(s["pt_act"], m + 1)
                    if ti:
                        pe.wait_ge(s["pt_dve"], m // 2 + 1)
                    pe.wait_ge(s["v_ready"], 4 * p + t + 1)
                    if m:
                        pe.wait_ge(s["o_lo"], m)
                    for c in range(ti + 1):
                        i = mm(ov[:], V[:, 2 * bb + c, g * D:(g + 1) * D], PTS[:, m % 2, c, :, :].rearrange("p h n -> p (h n)"),
                               start=(c == 0), stop=(c == ti))
                    i.then_inc(s["ov_full"], 1)
                elif st[0] == "F":
                    n = st[1]
                    p, g, bb = n // 8, (n // 2) % 4, n % 2
                    wst = ("split", "O", NKV * p + g)
                    wait_split(pe, wst)
                    pe.wait_ge(s["o_lo"], 2 * n + 2)
                    if n == 8:
                        pe.wait_ge(s["x1_ready"], 2)
                    for h in range(REP):
                        for mc in range(2):
                            w = wblock(wst, 256 * h + P * mc, 256 * h + P * mc + P)
                            i = three(acc[mc][:, T * bb:T * bb + T], w[0], w[1], OHs[:, h, :], OLs[:, h, :],
                                      g == 0 and bb == 0 and h == 0, g == NKV - 1 and h == REP - 1)
                    i.then_inc(s["wo_done"], 1)
                elif st[0] == "route":
                    _, p, k = st
                    if k in (2, 5):
                        continue
                    wait_proj_free(pe, st)
                    if k == 0:
                        wait_r(pe, 2 * p + 1, 2)
                        wait_split(pe, ("small",))
                        for ch in range(CH):
                            i = three(proj[:], GWH[:, ch, :], GWL[:, ch, :], RH[:, p, ch, :], RL[:, p, ch, :], ch == 0, ch == CH - 1)
                    elif k == 1:
                        pe.wait_ge(s["rt_act"], 6 * p + 1)
                        for t in range(TPP):
                            i = tp(proj[:, E * t:E * t + E], LT[:, P * t:P * t + P], ident[0:E, 0:E])
                    elif k == 3:
                        pe.wait_ge(s["rt_vec"], 6 * p + RT_VEC[2])
                        for t in range(TPP):
                            i = tp(proj[0:E, P * t:P * t + P], SC[:, t, :], ident)
                    elif k == 4:
                        pe.wait_ge(s["rt_act"], 6 * p + 3)
                        pe.wait_ge(s["onehot_ready"], 1)
                        for t in range(TPP):
                            i = mm(proj[:, E * t:E * t + E], LT[:, P * t:P * t + P], onehot[:], start=True, stop=True)
                    elif k == 6:
                        pe.wait_ge(s["rt_vec"], 6 * p + RT_VEC[5])
                        for t in range(TPP):
                            i = tp(proj[:, P * t:P * t + P], ST[:, t, :, :].rearrange("p d e -> p (d e)"), ident)
                    elif k == 7:
                        pe.wait_ge(s["zeros_ready"], 1)
                        for t in range(TPP):
                            i = tp(proj[0:64, P * t:P * t + P], STS[:, t, :], ident)
                    i.then_inc(s["proj_full"], 1)
                elif st[0] == "G":
                    f = st[1]
                    p, m = divmod(f, FT)
                    wst = ("split", "F", f)
                    wait_split(pe, wst)
                    wait_r(pe, 2 * p + 1, 2)
                    tok = slice(p * PT_, (p + 1) * PT_)
                    mcols = slice(P * m, P * m + P)
                    for a, bank in ((0, sc[f % 2]), (1, tr[f % 2])):
                        if a == 0:
                            if f >= 2:
                                pe.wait_ge(s["gate_used"], f - 1)
                            else:
                                pe.wait_ge(s["max_ready"], 48)
                        elif f >= 2:
                            pe.wait_ge(s["up_used"], f - 1)
                        else:
                            wait_turned(pe, len(TR_STEPS) - 1)
                            wait_turned(pe, len(TR_STEPS) - 2)
                        for ch in range(CH):
                            w = wblock(wst, 256 * a + P * ch, 256 * a + P * ch + P)
                            three(bank[:], w[0], w[1], RH[:, p, ch, :], RL[:, p, ch, :], ch == 0, False)
                        if a == 0:
                            pe.wait_ge(s["rt_vec"], 6 * p + 5)
                            if f == 0:
                                pe.wait_ge(s["table_lo"], G)
                        mm(bank[:], EXH[:, a, mcols], SX[:, tok], start=False, stop=False, skip_group_check=True)
                        i = mm(bank[:], EXL[:, a, mcols], SX[0:64, tok], start=False, stop=True, skip_group_check=True)
                        i.then_inc(s["gate_full" if a == 0 else "up_full"], 1)
                    if f:
                        pe.wait_ge(s["a_ready"], f)
                    else:
                        pe.wait_ge(s["o_lo"], 32)
                        pe.wait_ge(s["indicator_ready"], 1)
                    pe.wait_ge(s["rt_vec"], 6 * p + 6)
                    mm(ov[:], IND[:, mcols], SCX[:, tok], start=True, stop=True).then_inc(s["scal_full"], 1)
                elif st[0] == "Y":
                    f = st[1]
                    p, m = divmod(f, FT)
                    wst = ("split", "F", f)
                    pe.wait_ge(s["a_lo"], f + 1)
                    if f == 0:
                        pe.wait_ge(s["x1_ready"], 4)
                    if f == FT:
                        pe.wait_ge(s["result_ready"], 2)
                    sl = slice(512 * (f % 2), 512 * (f % 2) + 512)
                    for mc in range(2):
                        w = wblock(wst, 512 + P * mc, 512 + P * mc + P)
                        i = three(acc[mc][:], w[0], w[1], OH[:, sl], OL[:, sl], m == 0, m == FT - 1)
                    i.then_inc(s["ffn_used"], 1)


def kernel(**inputs):
    import numpy as np
    import concourse.bacc as bacc
    from concourse.bass_utils import run_bass_kernel_spmd

    def chunked(w):
        return np.ascontiguousarray(w.T.reshape(CH, P, -1).transpose(1, 0, 2))

    i = {k: np.asarray(v) for k, v in inputs.items()}
    f32 = np.float32
    a = {}
    a["xT"] = np.ascontiguousarray(i["x"].transpose(2, 0, 1).reshape(CH, P, B * T).transpose(1, 0, 2))
    a["fT"] = np.ascontiguousarray(i["fside_BxSxS_0"].transpose(2, 0, 1).reshape(CH, P, B * T).transpose(1, 0, 2))
    a["cond"] = np.ascontiguousarray(np.broadcast_to(i["cond_512"][None], (P, B, 64)))
    cv = [i[n].reshape(CH, P).T for n in ("L0_cond_w", "L0_cond_u", "L0_cond2_w", "L0_cond2_u")]
    cv += [i["L0_attn_q_scale"].reshape(P, 1), i["L0_attn_k_scale"].reshape(P, 1)]
    a["vecs"] = np.ascontiguousarray(np.concatenate(cv, axis=1))
    tri = np.where(np.arange(P)[None, :] <= np.arange(P)[:, None], 0.0, NEG_BIG).astype(f32)
    a["const"] = np.concatenate([np.eye(P, dtype=f32), np.zeros((P, P), f32), tri, np.arange(P, dtype=f32)[:, None]], axis=1)
    ind = np.zeros((64, FT * P), f32)
    for g in range(G):
        ind[g, g * FI:(g + 1) * FI] = 1.0
        ind[32 + g, g * FI:(g + 1) * FI] = 1.0
    a["ind"] = ind
    a["imap"] = np.ascontiguousarray(np.broadcast_to(i["L0_ffn_inv_map"].reshape(1, E), (E, E))).astype(np.int32)
    a["mup"] = np.ascontiguousarray(i["L0_ffn_mask_up_w"].transpose(1, 0, 2).reshape(CH, P, E).transpose(1, 0, 2))
    a["wk"] = chunked(i["L0_attn_Wk"]).reshape(P, 1024)
    a["wv"] = chunked(i["L0_attn_Wv"]).reshape(P, 1024)
    a["wq"] = np.ascontiguousarray(chunked(i["L0_attn_Wq"]).reshape(P, CH, NKV, REP * D).transpose(2, 0, 1, 3)).reshape(NKV, P, 1024)
    a["wo"] = np.ascontiguousarray(i["L0_attn_Wo"].T.reshape(NKV, REP, D, C).transpose(0, 2, 1, 3)).reshape(NKV, P, 1024)
    gate = np.zeros((P, CH, P), f32)
    gate[:, :, 0:E] = chunked(i["L0_ffn_gate_w"])
    a["gate"] = gate.reshape(P, CH * P)
    gp, up = (chunked(i[n].reshape(G * FI, C)) for n in ("L0_ffn_gate_proj_w", "L0_ffn_up_proj_w"))
    both = np.stack([gp, up], axis=1)
    a["tables"] = np.ascontiguousarray(both.reshape(P, 2, CH, G, FI).transpose(3, 0, 1, 2, 4)).reshape(G, P, 4 * FI)
    down = i["L0_ffn_down_proj_w"].transpose(0, 2, 1).reshape(FT, P, C)
    tiles = both.reshape(P, 2, CH, FT, P).transpose(3, 0, 1, 2, 4).reshape(FT, P, 512)
    a["ffn"] = np.ascontiguousarray(np.concatenate([tiles, down], axis=2))

    nc = bacc.Bacc("TRN2", target_bir_lowering=False, num_devices=1)
    arrays, ins = {}, {}
    for name, x in a.items():
        arrays[f"in_{name}"] = x
        ins[name] = nc.dram_tensor(f"in_{name}", x.shape, mybir.dt.from_np(x.dtype), kind="ExternalInput").ap()
    out = nc.dram_tensor("out_0", (P, CH, B * T), F32, kind="ExternalOutput").ap()
    program(nc, ins, out)
    r = run_bass_kernel_spmd(nc, [arrays], core_ids=[0])
    y = r.results[0]["out_0"]
    return y.transpose(1, 0, 2).reshape(C, B, T).transpose(1, 2, 0)
```
